# Optimizing a Trainium2 kernel written in Bass

```python
import numpy as np
import jax
import jax.numpy as jnp

def _softmax(x, axis=-1):
    return jax.nn.softmax(x, axis=axis)

def _gelu(x):
    return jax.nn.gelu(x, approximate=True)

def _silu(x):
    return jax.nn.silu(x)

def _sigmoid(x):
    return jax.nn.sigmoid(x)

def _layernorm(x, axis=-1, eps=1e-05):
    m = jnp.mean(x, axis=axis, keepdims=True)
    v = jnp.var(x, axis=axis, keepdims=True)
    return (x - m) / jnp.sqrt(v + eps)

def _scatter_add(tgt, idx, src, axis=0):
    return tgt.at[idx].add(src)

def _segment_sum(src, seg, n):
    return jax.ops.segment_sum(src, seg, n)
kernel_name = 'mk_rec_standalone_d1_rec_r8_8dce69'

def setup_inputs(seed: int=0):
    np.random.seed(seed)
    _w = jnp.asarray

    def _rec_inputs():
        import jax
        import jax.numpy as jnp
        _rk = jax.random.key(seed)
        r_inputs = -0.000520686 + 1.00062 * jax.random.normal(jax.random.fold_in(_rk, 1), (512, 32, 32), jnp.float32)
        return r_inputs
    r_inputs = _rec_inputs()

    def _L0_rec_setup():
        import jax, jax.numpy as jnp
        import numpy as np
        B, N, K = (256, 32, 32)
        CIN_SIZE = [128, 128]
        key = jax.random.key(seed)
        k1, k2, k3 = jax.random.split(key, 3)
        inputs = jax.random.normal(k1, (B, N, K), dtype=jnp.float32)
        W0 = jax.random.normal(k2, (N * N, CIN_SIZE[0]), dtype=jnp.float32) * 0.04
        W1 = jax.random.normal(k3, (N * CIN_SIZE[0], CIN_SIZE[1]), dtype=jnp.float32) * 0.02
        return {'inputs': inputs, 'W0': W0, 'W1': W1}
    _L0_rec_all = _L0_rec_setup()
    _L0_rec_in = {k: v for k, v in _L0_rec_all.items() if k in ('W0', 'W1')}
    del _L0_rec_all
    return {'r_inputs': r_inputs, 'L0_rec_W0': _L0_rec_in['W0'], 'L0_rec_W1': _L0_rec_in['W1']}

def reference(r_inputs, L0_rec_W0, L0_rec_W1):
    import jax
    import jax.numpy as jnp

    def _L0_rec_ref(inputs, W0, W1):
        import jax, jax.numpy as jnp
        import numpy as np
        B, N, K = (256, 32, 32)
        CIN_SIZE = [128, 128]
        b, n, k = inputs.shape
        x = inputs
        res = []
        for W in (W0, W1):
            prev = x.shape[1]
            z = jnp.einsum('bhd,bmd->bhmd', inputs, x).reshape(b, n * prev, k)
            x = jnp.einsum('bpd,pj->bjd', z, W)
            res.append(x)
        out = jnp.sum(jnp.concatenate(res, axis=1), axis=-1)
        return out
    y = _L0_rec_ref(r_inputs, L0_rec_W0, L0_rec_W1)
    return y

_drawn_inputs = setup_inputs


def setup_inputs(seed=0):
    import zlib

    import numpy as np

    out = dict(_drawn_inputs(seed))
    spreads = {}
    factors = {}
    for name, (base, spread) in spreads.items():
        noise = np.random.default_rng([zlib.crc32(name.encode()), seed]).standard_normal(out[name].shape)
        drawn = base * np.exp(spread * noise) if base else spread * noise
        out[name] = jnp.asarray(drawn.astype(out[name].dtype))
    for name, factor in factors.items():
        out[name] = (out[name] * factor).astype(out[name].dtype)
    return out
```

```python
from contextlib import ExitStack

import concourse.bass as bass
from concourse import mybir

F32 = mybir.dt.float32
ALU = mybir.AluOpType
ACT = mybir.ActivationFunctionType

P = 128
BATCH, FIELDS, DIMS = 512, 32, 32
J = 128
LANES = P // FIELDS
GROUP_B = P // DIMS
STEP_GROUPS = 4
STEP_B = GROUP_B * STEP_GROUPS
STEP_COLS = STEP_B * DIMS
STEPS = BATCH // STEP_B
CHUNK_B = P
CHUNK_STEPS = CHUNK_B // STEP_B
CHUNKS = BATCH // CHUNK_B
PAIRS = CHUNK_STEPS // 2

VIEW_START = [0, 12, 1, 0]
VIEW_STEP = [0, 1, 2, 2]
VIEWS = len(VIEW_START)
TILE_VIEWS = [(0, 1), (0, 2), (0, 3), (1, 2)]
TILES = len(TILE_VIEWS)
DIAGONAL = 2
TABLE_ROWS = FIELDS + max(a + s * (LANES - 1) for a, s in zip(VIEW_START, VIEW_STEP))

GCOLS = (FIELDS + 1) * GROUP_B
TAIL_COLS = 3 * P


def field_of(view, r, lane):
    return (r + VIEW_START[view] + lane * VIEW_STEP[view]) % FIELDS


def cin_kernel(nc, x_table, x_tail, w0_upper, w0_lower, w0_last, w1, out):
    with ExitStack() as ctx:
        def sb(name, shape, dt=F32):
            return ctx.enter_context(nc.sbuf_tensor(name, shape, dt))

        def sem(name):
            return ctx.enter_context(nc.semaphore(name))

        views = [sb(f"views{p}", [P, VIEWS, STEP_COLS]) for p in range(2)]
        tail = [sb(f"tail{p}", [P, 3, P]) for p in range(2)]
        z = [sb(f"z{p}", [P, TILES, STEP_COLS]) for p in range(2)]
        z_last = [sb(f"z_last{p}", [P, P]) for p in range(2)]
        xblock = [sb(f"xblock{p}", [P, STEP_GROUPS, FIELDS + 1, GROUP_B]) for p in range(2)]
        w0_sb = sb("w0_sb", [P, TILES, J])
        w0_low_sb = sb("w0_low_sb", [P, TILES, J])
        w0_last_sb = sb("w0_last_sb", [P, J])
        w1_sb = sb("w1_sb", [P, FIELDS, J])
        x1_sb = sb("x1_sb", [P, STEP_GROUPS, J])
        g_sb = sb("g_sb", [P, FIELDS + 1, CHUNK_B])
        ident = sb("ident", [P, P])
        out_sb = sb("out_sb", [P, 2 * J])

        x1_ps = [ctx.enter_context(nc.psum_tensor(f"x1_ps{g}", [P, 512], F32)) for g in range(STEP_GROUPS)]
        g_ps = [ctx.enter_context(nc.psum_tensor(f"g_ps{k}", [P, 512], F32)) for k in range(2)]
        out_ps = ctx.enter_context(nc.psum_tensor("out_ps", [P, 512], F32))

        views_loaded = [sem(f"views_loaded{p}") for p in range(2)]
        tail_loaded = [sem(f"tail_loaded{p}") for p in range(2)]
        w0_loaded = sem("w0_loaded")
        w1_loaded = sem("w1_loaded")
        w0_cleared = sem("w0_cleared")
        w0_folded = sem("w0_folded")
        constants_made = sem("constants_made")
        z_made = sem("z_made")
        xblock_made = sem("xblock_made")
        x1_done = sem("x1_done")
        x1_copied = sem("x1_copied")
        g_done = sem("g_done")
        g_copied = sem("g_copied")
        out_done = sem("out_done")
        out_copied = sem("out_copied")
        out_stored = sem("out_stored")
        sp_turns = sem("sp_turns")
        pool_turns = sem("pool_turns")
        Z_STEP = 1 + TILES
        CONSTANTS = 1 + 1 + 2 + 2 * GROUP_B
        W0_LOADS = 1 + 2 + (LANES - 1) + 1

        block = ctx.enter_context(nc.Block())

        @block.sync
        def _(sp):
            def load_step(step, column, p):
                for v in range(VIEWS):
                    rows = bass.AP(x_table.tensor, x_table.offset + VIEW_START[v] * BATCH * DIMS + column,
                                   [[BATCH * DIMS, FIELDS], [VIEW_STEP[v] * BATCH * DIMS, LANES], [1, STEP_COLS]])
                    sp.dma_start(views[p][:, v, :], rows).then_inc(views_loaded[p], 16)
                sp.dma_start(tail[p][:, :, :].rearrange("p k c -> p (k c)"), x_tail[step, :, :])\
                    .then_inc(tail_loaded[p], 16)

            for p in range(2):
                load_step(p, p * STEP_COLS, p)
            with sp.Fori(1, STEPS // 2) as i:
                for p in range(2):
                    step = i * 2 + p
                    column = step * STEP_COLS
                    sp.wait_ge(z_made, (step - 1) * Z_STEP).then_inc(sp_turns, 1)
                    sp.wait_ge(xblock_made, (step - 1) * GROUP_B).then_inc(sp_turns, 1)
                    load_step(step, column, p)

        @block.gpsimd
        def _(pool):
            pool.memset(w0_low_sb[:, :, :], 0.0).then_inc(w0_cleared, 1)
            pool.memset(ident[:, :], 0.0).then_inc(constants_made, 1)
            for p in range(2):
                pool.memset(xblock[p][:, :, :, :], 0.0).then_inc(constants_made, 1)
            pool.wait_ge(constants_made, 3)
            pool.affine_select(out=ident[:, :], in_=ident[:, :], compare_op=ALU.not_equal, fill=1.0,
                               base=0, pattern=[[-1, P]], channel_multiplier=1).then_inc(constants_made, 1)
            for p in range(2):
                for b in range(GROUP_B):
                    pool.wait_ge(constants_made, 4 + p * GROUP_B + b)
                    pool.memset(xblock[p][b * DIMS:(b + 1) * DIMS, :, FIELDS, b:b + 1], 1.0)\
                        .then_inc(constants_made, 1)

            def block_diagonal(step, p, i, first):
                pool.wait_ge(tail_loaded[p], i * 16 + 16).then_inc(pool_turns, 1)
                if not first:
                    pool.wait_ge(g_done, (step - 1) * 2).then_inc(pool_turns, 1)
                else:
                    pool.wait_ge(constants_made, CONSTANTS)
                for b in range(GROUP_B):
                    rows = slice(b * DIMS, (b + 1) * DIMS)
                    if not first or p or b:
                        pool.wait_ge(xblock_made, step * GROUP_B + b).then_inc(pool_turns, 1)
                    pool.tensor_copy(xblock[p][rows, :, 0:FIELDS, b],
                                     tail[p][rows, 2, :].rearrange("p (g h) -> p g h", g=STEP_GROUPS))\
                        .then_inc(xblock_made, 1)

            for p in range(2):
                block_diagonal(p, p, 0, True)
            with pool.Fori(1, STEPS // 2) as i:
                for p in range(2):
                    block_diagonal(i * 2 + p, p, i, False)

        @block.vector
        def _(dve):
            dve.wait_ge(w0_loaded, 16 * W0_LOADS)
            dve.tensor_tensor(w0_sb[:, :, :], w0_sb[:, :, :], w0_low_sb[:, :, :], ALU.add).then_inc(w0_folded, 1)

            def products(step, p, i, first):
                if not first:
                    dve.wait_ge(x1_done, (step - 1) * STEP_GROUPS)
                dve.wait_ge(tail_loaded[p], i * 16 + 16)
                dve.tensor_tensor(z_last[p][:, :], tail[p][:, 0, :], tail[p][:, 1, :], ALU.mult).then_inc(z_made, 1)
                dve.wait_ge(views_loaded[p], (i + 1) * (16 * VIEWS))
                for t, (a, b) in enumerate(TILE_VIEWS):
                    dve.tensor_tensor(z[p][:, t, :], views[p][:, a, :], views[p][:, b, :], ALU.mult)\
                        .then_inc(z_made, 1)

            for p in range(2):
                products(p, p, 0, True)
            with dve.Fori(1, STEPS // 2) as i:
                for p in range(2):
                    products(i * 2 + p, p, i, False)

        @block.scalar
        def _(act):
            act.dma_start(w0_sb[:, :, :].rearrange("p t j -> p (t j)"), w0_upper).then_inc(w0_loaded, 16)
            act.wait_ge(w0_cleared, 1)
            for tiles in (slice(0, DIAGONAL), slice(DIAGONAL + 1, TILES)):
                act.dma_start(w0_low_sb[:, tiles, :], w0_lower[:, tiles, :]).then_inc(w0_loaded, 16)
            for lane in range(1, LANES):
                act.dma_start(w0_low_sb[lane:lane + (FIELDS - 1) * LANES + 1:LANES, DIAGONAL, :],
                              w0_lower[lane:lane + (FIELDS - 1) * LANES + 1:LANES, DIAGONAL, :])\
                    .then_inc(w0_loaded, 16)
            act.dma_start(w0_last_sb[:, :], w0_last).then_inc(w0_loaded, 16)
            for k in range(4):
                act.dma_start(w1_sb[:, 8 * k:8 * k + 8, :], w1[:, 8 * k:8 * k + 8, :]).then_inc(w1_loaded, 16)

            def copies(step, chunk_step):
                for g in range(STEP_GROUPS):
                    act.wait_ge(x1_done, step * STEP_GROUPS + g + 1)
                    act.activation(x1_sb[:, g, :], x1_ps[g][:, 0:J], ACT.Copy).then_inc(x1_copied, 1)
                for k in range(2):
                    act.wait_ge(g_done, step * 2 + k + 1)
                    source = g_ps[k][:, 0:2 * GCOLS].rearrange("p (g h b) -> p h g b", g=2, b=GROUP_B)
                    target = g_sb[:, :, bass.ds(chunk_step * STEP_B + k * 2 * GROUP_B, 2 * GROUP_B)]
                    act.activation(target.rearrange("p h (g b) -> p h g b", g=2), source, ACT.Copy)\
                        .then_inc(g_copied, 1)

            def chunk(c, first):
                with act.Fori(0, PAIRS) as i:
                    for p in range(2):
                        copies(c * CHUNK_STEPS + i * 2 + p, i * 2 + p)
                act.wait_ge(out_done, c + 1)
                if not first:
                    act.wait_ge(out_stored, c * 16)
                act.activation(out_sb[:, :], out_ps[:, 0:2 * J], ACT.Copy).then_inc(out_copied, 1)
                act.wait_ge(out_copied, c + 1)
                act.dma_start(out[bass.ds(c * CHUNK_B, CHUNK_B), :], out_sb[:, :]).then_inc(out_stored, 16)

            chunk(0, True)
            with act.Fori(1, CHUNKS) as c:
                chunk(c, False)
            act.wait_ge(out_stored, 16 * CHUNKS)

        @block.tensor
        def _(pe):
            def layer0(step, p):
                pe.wait_ge(z_made, step * Z_STEP + 1)
                for g in range(STEP_GROUPS):
                    rows = slice(g * FIELDS, (g + 1) * FIELDS)
                    pe.matmul(x1_ps[g][:, 0:J], z_last[p][rows, :], w0_last_sb[rows, :], start=True, stop=False)
                pe.wait_ge(z_made, step * Z_STEP + Z_STEP)
                for g in range(STEP_GROUPS):
                    for t in range(TILES):
                        last = pe.matmul(x1_ps[g][:, 0:J], z[p][:, t, g * P:(g + 1) * P], w0_sb[:, t, :],
                                         start=False, stop=(t == TILES - 1))
                        if t == TILES - 1:
                            last.then_inc(x1_done, 1)

            def layer1_gram(step, p, first):
                pe.wait_ge(xblock_made, (step + 1) * GROUP_B)
                for g in range(STEP_GROUPS):
                    if g % 2 == 0 and not first:
                        pe.wait_ge(g_copied, step * 2 - 1 + g // 2)
                    pe.wait_ge(x1_copied, step * STEP_GROUPS + g + 1)
                    last = pe.matmul(g_ps[g // 2][:, (g % 2) * GCOLS:(g % 2 + 1) * GCOLS], x1_sb[:, g, :],
                                     xblock[p][:, g, :, :].rearrange("p h b -> p (h b)"), start=True, stop=True)
                    if g % 2 == 1:
                        last.then_inc(g_done, 1)

            def output(c, first):
                pe.wait_ge(g_copied, (c + 1) * (2 * CHUNK_STEPS))
                if first:
                    pe.wait_ge(w1_loaded, 64)
                else:
                    pe.wait_ge(out_copied, c)
                pe.matmul(out_ps[:, 0:J], g_sb[:, FIELDS, :], ident[:, :], start=True, stop=True)
                for h in range(FIELDS):
                    last = pe.matmul(out_ps[:, J:2 * J], g_sb[:, h, :], w1_sb[:, h, :],
                                     start=(h == 0), stop=(h == FIELDS - 1))
                last.then_inc(out_done, 1)

            def step_pair(first_step, first=False):
                for p in range(2):
                    step = first_step + p
                    layer0(step, p)
                    layer1_gram(step, p, first and p == 0)

            pe.wait_ge(w0_folded, 1)
            pe.wait_ge(w0_loaded, 16 * W0_LOADS)
            pe.wait_ge(constants_made, CONSTANTS)
            step_pair(0, True)
            with pe.Fori(1, PAIRS) as i:
                step_pair(i * 2)
            output(0, True)
            with pe.Fori(1, CHUNKS) as c:
                with pe.Fori(0, PAIRS) as i:
                    step_pair(c * CHUNK_STEPS + i * 2)
                output(c, False)


def kernel(r_inputs, L0_rec_W0, L0_rec_W1):
    import numpy as np
    import concourse.bacc as bacc
    from concourse.bass_utils import run_bass_kernel_spmd

    x = np.ascontiguousarray(r_inputs)
    x_rows = x.transpose(1, 0, 2).reshape(FIELDS, BATCH * DIMS)
    table = x_rows[[f % FIELDS for f in range(TABLE_ROWS)]]
    grouped = x.reshape(STEPS, STEP_GROUPS, GROUP_B, FIELDS, DIMS)
    factor = grouped.transpose(0, 1, 3, 2, 4)
    partner = factor[:, :, [(f + FIELDS // 2) % FIELDS for f in range(FIELDS)]]
    x_by_dim = grouped.transpose(0, 2, 4, 1, 3)
    tail = np.concatenate([factor.reshape(STEPS, P, P), partner.reshape(STEPS, P, P),
                           x_by_dim.reshape(STEPS, P, P)], axis=2)
    w0 = np.asarray(L0_rec_W0)
    rows = [(r, lane) for r in range(FIELDS) for lane in range(LANES)]
    upper = [[field_of(a, r, l) * FIELDS + field_of(b, r, l) for a, b in TILE_VIEWS] for r, l in rows]
    lower = [[field_of(b, r, l) * FIELDS + field_of(a, r, l) for a, b in TILE_VIEWS] for r, l in rows]
    last = [r * FIELDS + (r + FIELDS // 2) % FIELDS for _ in range(STEP_GROUPS) for r in range(FIELDS)]
    arrays = {
        "x_table": table,
        "x_tail": tail,
        "w0_upper": w0[upper].reshape(P, TILES * J),
        "w0_lower": w0[lower],
        "w0_last": w0[last],
        "w1": np.asarray(L0_rec_W1).reshape(FIELDS, P, J).transpose(1, 0, 2),
    }
    arrays = {name: np.ascontiguousarray(a) for name, a in arrays.items()}

    nc = bacc.Bacc("TRN2", target_bir_lowering=False, num_devices=1)
    args = [nc.dram_tensor(name, a.shape, F32, kind="ExternalInput").ap() for name, a in arrays.items()]
    out = nc.dram_tensor("out", (BATCH, 2 * J), F32, kind="ExternalOutput").ap()
    cin_kernel(nc, *args, out)
    result = run_bass_kernel_spmd(nc, [arrays], core_ids=[0])
    return result.results[0]["out"]
```

```python
from contextlib import ExitStack

import concourse.bass as bass
from concourse import mybir

F32 = mybir.dt.float32
F32R = mybir.dt.float32r
ALU = mybir.AluOpType
ACT = mybir.ActivationFunctionType

P = 128
BATCH, FIELDS, DIMS = 512, 32, 32
J = 128
LANES = P // FIELDS
GROUP_B = P // DIMS
STEP_GROUPS = 4
STEP_B = GROUP_B * STEP_GROUPS
STEP_COLS = STEP_B * DIMS
STEPS = BATCH // STEP_B
CHUNK_B = P
CHUNK_STEPS = CHUNK_B // STEP_B
CHUNKS = BATCH // CHUNK_B
PAIRS = CHUNK_STEPS // 2

VIEW_START = [0, 12, 1, 0]
VIEW_STEP = [0, 1, 2, 2]
VIEWS = len(VIEW_START)
TILE_VIEWS = [(0, 1), (0, 2), (0, 3), (1, 2)]
TILES = len(TILE_VIEWS)
DIAGONAL = 2
TABLE_ROWS = FIELDS + max(a + s * (LANES - 1) for a, s in zip(VIEW_START, VIEW_STEP))
SPLIT_TILES = 3

HALVES = 2
TERMS = 4
LAST_PAIRS = FIELDS // 2
LAST_ROWS = TERMS * LAST_PAIRS
LAST_COLS = STEP_COLS // HALVES

GCOLS = (FIELDS + 1) * GROUP_B
W1_LOADS = 4


def field_of(view, r, lane):
    return (r + VIEW_START[view] + lane * VIEW_STEP[view]) % FIELDS


def cin_kernel(nc, x_table, x_last, x_dims, w0_upper, w0_lower, w0_last, signs, w1, out):
    with ExitStack() as ctx:
        def sb(name, shape, dt=F32):
            return ctx.enter_context(nc.sbuf_tensor(name, shape, dt))

        def sem(name):
            return ctx.enter_context(nc.semaphore(name))

        views = [sb(f"views{p}", [P, VIEWS, STEP_COLS]) for p in range(2)]
        factors = [sb(f"factors{p}", [P, 2, LAST_COLS]) for p in range(2)]
        z = [sb(f"z{p}", [P, TILES, STEP_COLS]) for p in range(2)]
        z_high = [sb(f"z_high{p}", [P, SPLIT_TILES, STEP_COLS], F32R) for p in range(2)]
        z_low = [sb(f"z_low{p}", [P, SPLIT_TILES, STEP_COLS], F32R) for p in range(2)]
        z_last = [sb(f"z_last{p}", [P, LAST_COLS]) for p in range(2)]
        z_last_high = [sb(f"z_last_high{p}", [P, LAST_COLS], F32R) for p in range(2)]
        z_last_terms = [sb(f"z_last_terms{p}", [P, LAST_COLS], F32R) for p in range(2)]
        xblock = [sb(f"xblock{p}", [P, STEP_GROUPS, FIELDS + 1, GROUP_B]) for p in range(2)]
        x_by_dim = sb("x_by_dim", [P, STEPS, STEP_GROUPS, FIELDS])
        x1_sb = sb("x1_sb", [P, STEP_COLS])
        x1_turned = sb("x1_turned", [P, STEP_GROUPS, J])
        g_sb = sb("g_sb", [P, FIELDS + 1, CHUNK_B])
        out_sb = sb("out_sb", [P, 2 * J])
        w0_sb = sb("w0_sb", [P, TILES, J])
        w0_lower_sb = sb("w0_lower_sb", [P, TILES, J])
        w0_high = sb("w0_high", [P, SPLIT_TILES, J], F32R)
        w0_low = sb("w0_low", [P, SPLIT_TILES, J], F32R)
        w0_last_sb = sb("w0_last_sb", [P, 2, J])
        w0_last_sum = sb("w0_last_sum", [P, J])
        w0_last_high = sb("w0_last_high", [P, J], F32R)
        w0_last_terms = sb("w0_last_terms", [P, HALVES, J], F32R)
        signs_sb = sb("signs_sb", [P, 2])
        w1_sb = sb("w1_sb", [P, FIELDS, J])
        ident = sb("ident", [P, P])

        x1_ps = [ctx.enter_context(nc.psum_tensor(f"x1_ps{p}", [P, STEP_COLS], F32)) for p in range(2)]
        turned_ps = ctx.enter_context(nc.psum_tensor("turned_ps", [P, STEP_GROUPS, J], F32))
        g_ps = [ctx.enter_context(nc.psum_tensor(f"g_ps{k}", [P, 512], F32)) for k in range(2)]
        out_ps = ctx.enter_context(nc.psum_tensor("out_ps", [P, 512], F32))

        views_loaded = [[sem(f"view{v}_loaded{p}") for v in range(VIEWS)] for p in range(2)]
        factors_loaded = [sem(f"factors_loaded{p}") for p in range(2)]
        x_by_dim_begun = sem("x_by_dim_begun")
        x_by_dim_loaded = sem("x_by_dim_loaded")
        w0_loaded = sem("w0_loaded")
        w1_loaded = sem("w1_loaded")
        w0_cleared = sem("w0_cleared")
        w0_folded = sem("w0_folded")
        w0_highs = sem("w0_highs")
        w0_lows = sem("w0_lows")
        constants_made = sem("constants_made")
        z_made = sem("z_made")
        z_highs = sem("z_highs")
        z_lows = sem("z_lows")
        xblock_made = sem("xblock_made")
        z_whole_used = sem("z_whole_used")
        x1_done = sem("x1_done")
        x1_copied = sem("x1_copied")
        x1_was_turned = sem("x1_was_turned")
        turned_copied = sem("turned_copied")
        g_done = sem("g_done")
        g_copied = sem("g_copied")
        out_done = sem("out_done")
        out_copied = sem("out_copied")
        out_stored = sem("out_stored")
        sp_turns = sem("sp_turns")
        pool_turns = sem("pool_turns")
        Z_OPS = 4
        PARTS = 3
        CONSTANTS = 1 + 2 + 1 + 2 * GROUP_B
        W0_FILLS = 2
        W0_LOADS = 1 + 2 + (LANES - 1) + 2

        block = ctx.enter_context(nc.Block())

        @block.sync
        def _(sp):
            def load_view(v, column, p):
                rows = bass.AP(x_table.tensor, x_table.offset + VIEW_START[v] * BATCH * DIMS + column,
                               [[BATCH * DIMS, FIELDS], [VIEW_STEP[v] * BATCH * DIMS, LANES], [1, STEP_COLS]])
                sp.dma_start(views[p][:, v, :], rows).then_inc(views_loaded[p][v], 16)

            def load_factors(step, p):
                sp.dma_start(factors[p][:, :, :].rearrange("p k c -> p (k c)"), x_last[step, :, :])\
                    .then_inc(factors_loaded[p], 16)

            def load_pair(i):
                for p in range(2):
                    step = i * 2 + p
                    used = (step - 2) * Z_OPS
                    sp.wait_ge(z_made, used + 2).then_inc(sp_turns, 1)
                    for v in (0, 3):
                        load_view(v, step * STEP_COLS, p)
                    sp.wait_ge(z_made, used + 3).then_inc(sp_turns, 1)
                    for v in (1, 2):
                        load_view(v, step * STEP_COLS, p)
                    sp.wait_ge(z_made, used + 4).then_inc(sp_turns, 1)
                    load_factors(step, p)

            for p in range(2):
                for v in range(VIEWS):
                    load_view(v, p * STEP_COLS, p)
                load_factors(p, p)
                if p == 0:
                    sp.dma_start(x_by_dim[:, 0:CHUNK_STEPS, :, :].rearrange("p s g h -> p (s g h)"),
                                 x_dims[:, 0:CHUNK_STEPS * P]).then_inc(x_by_dim_begun, 16)
            load_pair(1)
            sp.dma_start(x_by_dim[:, CHUNK_STEPS:, :, :].rearrange("p s g h -> p (s g h)"),
                         x_dims[:, CHUNK_STEPS * P:]).then_inc(x_by_dim_loaded, 16)
            with sp.Fori(2, STEPS // 2) as i:
                load_pair(i)

        @block.gpsimd
        def _(pool):
            pool.memset(w0_lower_sb[:, DIAGONAL, :], 0.0).then_inc(w0_cleared, 1)
            pool.memset(w0_last_terms[:, :, :].bitcast(F32), 0.0).then_inc(w0_cleared, 1)
            pool.memset(ident[:, :], 0.0).then_inc(constants_made, 1)
            for p in range(2):
                pool.memset(xblock[p][:, :, :, :], 0.0).then_inc(constants_made, 1)
            pool.wait_ge(constants_made, 3)
            pool.affine_select(out=ident[:, :], in_=ident[:, :], compare_op=ALU.not_equal, fill=1.0,
                               base=0, pattern=[[-1, P]], channel_multiplier=1).then_inc(constants_made, 1)
            for p in range(2):
                for b in range(GROUP_B):
                    pool.wait_ge(constants_made, 4 + p * GROUP_B + b)
                    pool.memset(xblock[p][b * DIMS:(b + 1) * DIMS, :, FIELDS, b:b + 1], 1.0)\
                        .then_inc(constants_made, 1)

            def block_diagonal(step, p, first=False):
                if not first:
                    pool.wait_ge(g_done, (step - 1) * 2).then_inc(pool_turns, 1)
                for b in range(GROUP_B):
                    rows = slice(b * DIMS, (b + 1) * DIMS)
                    if not (first and p == 0 and b == 0):
                        pool.wait_ge(xblock_made, step * GROUP_B + b).then_inc(pool_turns, 1)
                    pool.tensor_copy(xblock[p][rows, :, 0:FIELDS, b], x_by_dim[rows, bass.ds(step, 1), :, :]
                                     .rearrange("p s g h -> p (s g) h")).then_inc(xblock_made, 1)

            pool.wait_ge(constants_made, CONSTANTS)
            pool.wait_ge(x_by_dim_begun, 16)
            for p in range(2):
                block_diagonal(p, p, first=True)
            with pool.Fori(1, PAIRS) as i:
                for p in range(2):
                    block_diagonal(i * 2 + p, p)
            pool.wait_ge(x_by_dim_loaded, 16)
            with pool.Fori(PAIRS, STEPS // 2) as i:
                for p in range(2):
                    block_diagonal(i * 2 + p, p)

        @block.vector
        def _(dve):
            def products(step, p, i, first):
                loaded = (i + 1) * 16
                for v in range(3):
                    dve.wait_ge(views_loaded[p][v], loaded)
                dve.tensor_tensor(z[p][:, 0:2, :], views[p][:, 0:1, :].broadcast_to([P, 2, STEP_COLS]),
                                  views[p][:, 1:3, :], ALU.mult).then_inc(z_made, 1)
                dve.wait_ge(views_loaded[p][3], loaded)
                dve.tensor_tensor(z[p][:, 2, :], views[p][:, 0, :], views[p][:, 3, :], ALU.mult).then_inc(z_made, 1)
                if not first:
                    dve.wait_ge(z_whole_used, step - 1)
                dve.tensor_tensor(z[p][:, 3, :], views[p][:, 1, :], views[p][:, 2, :], ALU.mult).then_inc(z_made, 1)
                dve.wait_ge(factors_loaded[p], loaded)
                dve.tensor_tensor(z_last[p][:, :], factors[p][:, 0, :], factors[p][:, 1, :], ALU.mult).then_inc(z_made, 1)

            def lows(step, p):
                for part, tiles in enumerate((slice(0, 2), slice(2, 3))):
                    dve.wait_ge(z_highs, step * PARTS + part + 1)
                    dve.tensor_tensor(z_low[p][:, tiles, :], z[p][:, tiles, :], z_high[p][:, tiles, :].bitcast(F32),
                                      ALU.subtract).then_inc(z_lows, 1)
                dve.wait_ge(z_highs, step * PARTS + PARTS)
                dve.scalar_tensor_tensor(out=z_last_terms[p][:, :], in0=z_last_high[p][:, :].bitcast(F32),
                                         scalar=signs_sb[:, 0:1], in1=z_last[p][:, :], op0=ALU.mult, op1=ALU.add)\
                    .then_inc(z_lows, 1)

            def fold_weights():
                dve.wait_ge(w0_loaded, 16 * W0_LOADS)
                dve.tensor_tensor(w0_sb[:, :, :], w0_sb[:, :, :], w0_lower_sb[:, :, :], ALU.add)\
                    .then_inc(w0_folded, 1)
                dve.tensor_tensor(w0_last_sum[:, :], w0_last_sb[:, 0, :], w0_last_sb[:, 1, :], ALU.add)\
                    .then_inc(w0_folded, 1)

            def weight_lows():
                dve.wait_ge(w0_highs, 2)
                dve.tensor_tensor(w0_low[:, :, :], w0_sb[:, 0:SPLIT_TILES, :], w0_high[:, :, :].bitcast(F32),
                                  ALU.subtract).then_inc(w0_lows, 1)
                dve.wait_ge(w0_cleared, W0_FILLS)
                for half in range(HALVES):
                    rows = slice(half * LAST_ROWS, (half + 1) * LAST_ROWS)
                    dve.scalar_tensor_tensor(out=w0_last_terms[rows, half, :], in0=w0_last_high[rows, :].bitcast(F32),
                                             scalar=signs_sb[rows, 1:2], in1=w0_last_sum[rows, :],
                                             op0=ALU.mult, op1=ALU.add).then_inc(w0_lows, 1)

            products(0, 0, 0, True)
            fold_weights()
            lows(0, 0)
            weight_lows()
            products(1, 1, 0, True)
            lows(1, 1)
            with dve.Fori(1, STEPS // 2) as i:
                for p in range(2):
                    products(i * 2 + p, p, i, False)
                    lows(i * 2 + p, p)

        @block.scalar
        def _(act):
            act.dma_start(w0_sb[:, :, :].rearrange("p t j -> p (t j)"), w0_upper).then_inc(w0_loaded, 16)
            for tiles in (slice(0, DIAGONAL), slice(DIAGONAL + 1, TILES)):
                act.dma_start(w0_lower_sb[:, tiles, :], w0_lower[:, tiles, :]).then_inc(w0_loaded, 16)
            act.dma_start(w0_last_sb[:, :, :], w0_last).then_inc(w0_loaded, 16)
            act.dma_start(signs_sb[:, :], signs).then_inc(w0_loaded, 16)
            act.wait_ge(w0_cleared, 1)
            for lane in range(1, LANES):
                act.dma_start(w0_lower_sb[lane:lane + (FIELDS - 1) * LANES + 1:LANES, DIAGONAL, :],
                              w0_lower[lane:lane + (FIELDS - 1) * LANES + 1:LANES, DIAGONAL, :])\
                    .then_inc(w0_loaded, 16)

            def highs(step, p, parts=range(PARTS)):
                for part in parts:
                    if part < PARTS - 1:
                        tiles = (slice(0, 2), slice(2, 3))[part]
                        act.wait_ge(z_made, step * Z_OPS + part + 1)
                        act.activation(z_high[p][:, tiles, :], z[p][:, tiles, :], ACT.Copy).then_inc(z_highs, 1)
                    else:
                        act.wait_ge(z_made, step * Z_OPS + Z_OPS)
                        act.activation(z_last_high[p][:, :], z_last[p][:, :], ACT.Copy).then_inc(z_highs, 1)

            def x1_copy(step, p):
                act.wait_ge(x1_done, step + 1)
                act.activation(x1_sb[:, :], x1_ps[p][:, :], ACT.Copy).then_inc(x1_copied, 1)

            def turned_copy(step):
                act.wait_ge(x1_was_turned, step + 1)
                act.activation(x1_turned[:, :, :], turned_ps[:, :, :], ACT.Copy).then_inc(turned_copied, 1)

            def g_copies(step, chunk_step):
                for k in range(2):
                    act.wait_ge(g_done, step * 2 + k + 1)
                    source = g_ps[k][:, 0:2 * GCOLS].rearrange("p (g h b) -> p h g b", g=2, b=GROUP_B)
                    target = g_sb[:, :, bass.ds(chunk_step * STEP_B + k * 2 * GROUP_B, 2 * GROUP_B)]
                    act.activation(target.rearrange("p h (g b) -> p h g b", g=2), source, ACT.Copy)\
                        .then_inc(g_copied, 1)

            def store(c, first=False):
                act.wait_ge(out_done, c + 1)
                if not first:
                    act.wait_ge(out_stored, c * 16)
                act.activation(out_sb[:, :], out_ps[:, 0:2 * J], ACT.Copy).then_inc(out_copied, 1)
                act.wait_ge(out_copied, c + 1)
                act.dma_start(out[bass.ds(c * CHUNK_B, CHUNK_B), :], out_sb[:, :]).then_inc(out_stored, 16)

            def turn(step, p, chunk_step, finished=None, first=False, last=False):
                if chunk_step is not None:
                    x1_copy(step - 1, 1 - p)
                if not last:
                    highs(step + 1, 1 - p, range(1))
                if chunk_step is not None:
                    turned_copy(step - 1)
                if not last:
                    highs(step + 1, 1 - p, range(1, PARTS))
                if finished is not None:
                    store(finished, first)
                if chunk_step is not None:
                    g_copies(step - 1, chunk_step)

            def chunk_start(c, first=False):
                turn(c * CHUNK_STEPS, 0, CHUNK_STEPS - 1)
                turn(c * CHUNK_STEPS + 1, 1, 0, finished=c - 1, first=first)

            def chunk_rest(c, pairs):
                with act.Fori(1, pairs) as i:
                    for p in range(2):
                        turn(c * CHUNK_STEPS + i * 2 + p, p, i * 2 + p - 1)

            highs(0, 0)
            act.wait_ge(w0_folded, 2)
            act.activation(w0_high[:, :, :], w0_sb[:, 0:SPLIT_TILES, :], ACT.Copy).then_inc(w0_highs, 1)
            act.activation(w0_last_high[:, :], w0_last_sum[:, :], ACT.Copy).then_inc(w0_highs, 1)
            for k in range(W1_LOADS):
                part = slice(k * FIELDS // W1_LOADS, (k + 1) * FIELDS // W1_LOADS)
                act.dma_start(w1_sb[:, part, :], w1[:, part, :]).then_inc(w1_loaded, 16)
            turn(0, 0, None)
            turn(1, 1, 0)
            chunk_rest(0, PAIRS)
            chunk_start(1, first=True)
            chunk_rest(1, PAIRS)
            with act.Fori(2, CHUNKS - 1) as c:
                chunk_start(c)
                chunk_rest(c, PAIRS)
            chunk_start(CHUNKS - 1)
            chunk_rest(CHUNKS - 1, PAIRS - 1)
            turn(STEPS - 2, 0, CHUNK_STEPS - 3)
            turn(STEPS - 1, 1, CHUNK_STEPS - 2, last=True)
            x1_copy(STEPS - 1, 1)
            turned_copy(STEPS - 1)
            g_copies(STEPS - 1, CHUNK_STEPS - 1)
            store(CHUNKS - 1)
            act.wait_ge(out_stored, 16 * CHUNKS)

        @block.tensor
        def _(pe):
            def split_tile(x1, p, t, start=False):
                pe.matmul(x1, w0_high[:, t, :], z_low[p][:, t, :], start=start, stop=False)
                pe.matmul(x1, w0_low[:, t, :], z_high[p][:, t, :], start=False, stop=False)
                pe.matmul(x1, w0_high[:, t, :], z_high[p][:, t, :], start=False, stop=False)

            def layer0_begin(step, p):
                pe.wait_ge(z_lows, step * PARTS + 1)
                split_tile(x1_ps[p][:, :], p, 0, start=True)
                pe.matmul(x1_ps[p][:, :], w0_sb[:, SPLIT_TILES, :], z[p][:, SPLIT_TILES, :], start=False, stop=False)\
                    .then_inc(z_whole_used, 1)

            def layer0_end(step, p):
                split_tile(x1_ps[p][:, :], p, 1)
                pe.wait_ge(z_lows, step * PARTS + PARTS)
                for t in range(2, SPLIT_TILES):
                    split_tile(x1_ps[p][:, :], p, t)
                for half in range(HALVES):
                    last = pe.matmul(x1_ps[p][:, half * LAST_COLS:(half + 1) * LAST_COLS], w0_last_terms[:, half, :],
                                     z_last_terms[p][:, :], start=False, stop=(half == HALVES - 1))
                last.then_inc(x1_done, 1)

            def turn_x1(step):
                pe.wait_ge(x1_copied, step + 1)
                for g in range(STEP_GROUPS):
                    last = pe.transpose(turned_ps[:, g, :], x1_sb[:, g * P:(g + 1) * P], ident[:, :])
                last.then_inc(x1_was_turned, 1)

            def layer1_gram(step, p, first):
                pe.wait_ge(xblock_made, (step + 1) * GROUP_B)
                pe.wait_ge(turned_copied, step + 1)
                for g in range(STEP_GROUPS):
                    if g % 2 == 0 and not first:
                        pe.wait_ge(g_copied, step * 2 - 1 + g // 2)
                    last = pe.matmul(g_ps[g // 2][:, (g % 2) * GCOLS:(g % 2 + 1) * GCOLS], x1_turned[:, g, :],
                                     xblock[p][:, g, :, :].rearrange("p h b -> p (h b)"), start=True, stop=True)
                    if g % 2 == 1:
                        last.then_inc(g_done, 1)

            def output(c, first=False):
                pe.wait_ge(g_copied, (c + 1) * (2 * CHUNK_STEPS))
                if first:
                    pe.wait_ge(w1_loaded, 16 * W1_LOADS)
                else:
                    pe.wait_ge(out_copied, c)
                pe.matmul(out_ps[:, 0:J], g_sb[:, FIELDS, :], ident[:, :], start=True, stop=True)
                for h in range(FIELDS):
                    last = pe.matmul(out_ps[:, J:2 * J], g_sb[:, h, :], w1_sb[:, h, :],
                                     start=(h == 0), stop=(h == FIELDS - 1))
                last.then_inc(out_done, 1)

            def turn(step, p, finished=None, first=False):
                layer0_begin(step, p)
                turn_x1(step - 1)
                layer0_end(step, p)
                if finished is not None:
                    output(finished, first)
                layer1_gram(step - 1, 1 - p, first and finished is None)

            def chunk_start(c, first=False):
                turn(c * CHUNK_STEPS, 0)
                turn(c * CHUNK_STEPS + 1, 1, finished=c - 1, first=first)

            def chunk_rest(c):
                with pe.Fori(1, PAIRS) as i:
                    for p in range(2):
                        turn(c * CHUNK_STEPS + i * 2 + p, p)

            pe.wait_ge(w0_lows, 1 + HALVES)
            pe.wait_ge(constants_made, CONSTANTS)
            layer0_begin(0, 0)
            layer0_end(0, 0)
            turn(1, 1, first=True)
            chunk_rest(0)
            chunk_start(1, first=True)
            chunk_rest(1)
            with pe.Fori(2, CHUNKS) as c:
                chunk_start(c)
                chunk_rest(c)
            turn_x1(STEPS - 1)
            layer1_gram(STEPS - 1, 1, False)
            output(CHUNKS - 1)


def kernel(r_inputs, L0_rec_W0, L0_rec_W1):
    import numpy as np
    import concourse.bacc as bacc
    from concourse.bass_utils import run_bass_kernel_spmd

    x = np.ascontiguousarray(r_inputs)
    x_rows = x.transpose(1, 0, 2).reshape(FIELDS, BATCH * DIMS)
    table = x_rows[[f % FIELDS for f in range(TABLE_ROWS)]]
    grouped = x.reshape(STEPS, HALVES, STEP_GROUPS // HALVES, GROUP_B, FIELDS, DIMS)
    by_field = grouped.transpose(0, 1, 4, 2, 3, 5).reshape(STEPS, HALVES, 1, FIELDS, LAST_COLS)
    shape = (STEPS, HALVES, TERMS, LAST_PAIRS, LAST_COLS)
    factor = np.broadcast_to(by_field[:, :, :, :LAST_PAIRS], shape)
    partner = np.broadcast_to(by_field[:, :, :, LAST_PAIRS:], shape)
    x_by_dim = x.reshape(STEPS, STEP_GROUPS, GROUP_B, FIELDS, DIMS).transpose(2, 4, 0, 1, 3)
    w0 = np.asarray(L0_rec_W0)
    rows = [(r, lane) for r in range(FIELDS) for lane in range(LANES)]
    upper = [[field_of(a, r, l) * FIELDS + field_of(b, r, l) for a, b in TILE_VIEWS] for r, l in rows]
    lower = [[field_of(b, r, l) * FIELDS + field_of(a, r, l) for a, b in TILE_VIEWS] for r, l in rows]
    last = [[i * FIELDS + i + LAST_PAIRS, (i + LAST_PAIRS) * FIELDS + i]
            for _ in range(HALVES * TERMS) for i in range(LAST_PAIRS)]
    signs = [[-float(term // 2), -float(term % 2)]
             for _ in range(HALVES) for term in range(TERMS) for _ in range(LAST_PAIRS)]
    arrays = {
        "x_table": table,
        "x_last": np.concatenate([factor.reshape(STEPS, P, LAST_COLS), partner.reshape(STEPS, P, LAST_COLS)], axis=2),
        "x_dims": x_by_dim.reshape(P, STEPS * P),
        "w0_upper": w0[upper].reshape(P, TILES * J),
        "w0_lower": w0[lower],
        "w0_last": w0[last],
        "signs": np.array(signs, np.float32),
        "w1": np.asarray(L0_rec_W1).reshape(FIELDS, P, J).transpose(1, 0, 2),
    }
    arrays = {name: np.ascontiguousarray(a) for name, a in arrays.items()}

    nc = bacc.Bacc("TRN2", target_bir_lowering=False, num_devices=1)
    args = [nc.dram_tensor(name, a.shape, F32, kind="ExternalInput").ap() for name, a in arrays.items()]
    out = nc.dram_tensor("out", (BATCH, 2 * J), F32, kind="ExternalOutput").ap()
    cin_kernel(nc, *args, out)
    result = run_bass_kernel_spmd(nc, [arrays], core_ids=[0])
    return result.results[0]["out"]
```

```python
from contextlib import ExitStack

import concourse.bass as bass
from concourse import mybir

F32 = mybir.dt.float32
F32R = mybir.dt.float32r
ALU = mybir.AluOpType
ACT = mybir.ActivationFunctionType

P = 128
BATCH, FIELDS, DIMS = 512, 32, 32
J = 128
LANES = P // FIELDS
GROUP_B = P // DIMS
STEP_GROUPS = 4
STEP_B = GROUP_B * STEP_GROUPS
STEP_COLS = STEP_B * DIMS
STEPS = BATCH // STEP_B
CHUNK_B = P
CHUNK_STEPS = CHUNK_B // STEP_B
CHUNKS = BATCH // CHUNK_B
PAIRS = CHUNK_STEPS // 2
SPLITS = (2, 3)

VIEW_START = [0, 12, 1, 0]
VIEW_STEP = [0, 1, 2, 2]
VIEWS = len(VIEW_START)
TILE_VIEWS = [(0, 1), (0, 2), (0, 3), (1, 2)]
TILES = len(TILE_VIEWS)
DIAGONAL = 2
TABLE_ROWS = FIELDS + max(a + s * (LANES - 1) for a, s in zip(VIEW_START, VIEW_STEP))
SPLIT_TILES = max(SPLITS)

HALVES = 2
TERMS = 4
LAST_PAIRS = FIELDS // 2
LAST_ROWS = TERMS * LAST_PAIRS
LAST_COLS = STEP_COLS // HALVES

GCOLS = (FIELDS + 1) * GROUP_B
W1_LOADS = CHUNK_STEPS
W1_FIELDS = FIELDS // W1_LOADS
REST_TILES = TILES - 1
W0_CONSTANTS = 2 * REST_TILES * J
SIGN_Z, SIGN_W, ONCE = range(3)
W0_REST_COLS = W0_CONSTANTS + 3
WARM_COLS = 256
WARM_PRODUCTS = 5


def field_of(view, r, lane):
    return (r + VIEW_START[view] + lane * VIEW_STEP[view]) % FIELDS


def cin_kernel(nc, x_table, x_last, x_dims, w0_tile3, w0_rest, w0_last, w1, out):
    with ExitStack() as ctx:
        def sb(name, shape, dt=F32):
            return ctx.enter_context(nc.sbuf_tensor(name, shape, dt))

        def sem(name):
            return ctx.enter_context(nc.semaphore(name))

        views = [sb(f"views{p}", [P, VIEWS, STEP_COLS]) for p in range(2)]
        factors = [sb(f"factors{p}", [P, 2, LAST_COLS]) for p in range(2)]
        z = [sb(f"z{p}", [P, TILES, STEP_COLS]) for p in range(2)]
        z_high = [sb(f"z_high{p}", [P, SPLIT_TILES, STEP_COLS], F32R) for p in range(2)]
        z_low = [sb(f"z_low{p}", [P, SPLIT_TILES, STEP_COLS], F32R) for p in range(2)]
        z_last = [sb(f"z_last{p}", [P, LAST_COLS]) for p in range(2)]
        z_last_high = [sb(f"z_last_high{p}", [P, LAST_COLS], F32R) for p in range(2)]
        z_last_terms = [sb(f"z_last_terms{p}", [P, LAST_COLS], F32R) for p in range(2)]
        xblock = [sb(f"xblock{p}", [P, STEP_GROUPS, FIELDS + 1, GROUP_B]) for p in range(2)]
        x_by_dim = sb("x_by_dim", [P, STEPS, STEP_GROUPS, FIELDS])
        x1_sb = sb("x1_sb", [P, STEP_COLS])
        x1_turned = sb("x1_turned", [P, STEP_GROUPS, J])
        g_sb = sb("g_sb", [P, FIELDS + 1, CHUNK_B])
        out_sb = sb("out_sb", [P, 2 * J])
        w0_tile3_sb = sb("w0_tile3_sb", [P, 2, J])
        w0_rest_sb = sb("w0_rest_sb", [P, W0_REST_COLS])
        w0_last_sb = sb("w0_last_sb", [P, 2, J])
        w0_tile3_sum = sb("w0_tile3_sum", [P, J])
        w0_sum = sb("w0_sum", [P, REST_TILES, J])
        w0_high = sb("w0_high", [P, SPLIT_TILES, J], F32R)
        w0_low = sb("w0_low", [P, SPLIT_TILES, J], F32R)
        w0_last_sum = sb("w0_last_sum", [P, J])
        w0_last_high = sb("w0_last_high", [P, J], F32R)
        w0_last_terms = sb("w0_last_terms", [P, HALVES, J], F32R)
        table_data = sb("table_data", [P, 2])
        zeros = sb("zeros", [P, WARM_COLS])
        w1_sb = sb("w1_sb", [P, FIELDS, J])
        ident = sb("ident", [P, P])

        x1_ps = [ctx.enter_context(nc.psum_tensor(f"x1_ps{p}", [P, STEP_COLS], F32)) for p in range(2)]
        turned_ps = ctx.enter_context(nc.psum_tensor("turned_ps", [P, STEP_GROUPS, J], F32))
        g_ps = [ctx.enter_context(nc.psum_tensor(f"g_ps{k}", [P, 512], F32)) for k in range(2)]
        out_ps = ctx.enter_context(nc.psum_tensor("out_ps", [P, 512], F32))

        HALF_GROUPS = STEP_GROUPS // HALVES
        turned_half_ps = [turned_ps[:, 0:HALF_GROUPS, :],
                          x1_ps[0][:, 0:LAST_COLS].rearrange("p (g j) -> p g j", j=J)]

        views_loaded = [[sem(f"view{v}_loaded{p}") for v in range(VIEWS)] for p in range(2)]
        factors_loaded = [sem(f"factors_loaded{p}") for p in range(2)]
        x_by_dim_loaded = sem("x_by_dim_loaded")
        w0_tile3_loaded = sem("w0_tile3_loaded")
        w0_rest_loaded = sem("w0_rest_loaded")
        w0_last_loaded = sem("w0_last_loaded")
        w1_loaded = sem("w1_loaded")
        w0_cleared = sem("w0_cleared")
        w0_added = sem("w0_added")
        w0_folded = sem("w0_folded")
        w0_last_folded = sem("w0_last_folded")
        w0_tile3_folded = sem("w0_tile3_folded")
        zeros_made = sem("zeros_made")
        table_input = sem("table_input")
        table_ready = sem("table_ready")
        w0_highs = sem("w0_highs")
        w0_lows = sem("w0_lows")
        constants_made = sem("constants_made")
        z_made = sem("z_made")
        z_highs = sem("z_highs")
        z_lows = sem("z_lows")
        xblock_made = sem("xblock_made")
        z_whole_used = sem("z_whole_used")
        x1_done = sem("x1_done")
        x1_copied = sem("x1_copied")
        x1_was_turned = sem("x1_was_turned")
        turned_copied = sem("turned_copied")
        g_done = sem("g_done")
        g_copied = sem("g_copied")
        out_done = sem("out_done")
        out_copied = sem("out_copied")
        out_stored = sem("out_stored")
        sp_turns = sem("sp_turns")
        Z_OPS = 4
        PARTS = 3
        CONSTANTS = 1 + 2 + 1 + 2 * GROUP_B

        block = ctx.enter_context(nc.Block())

        @block.sync
        def _(sp):
            def load_view(v, column, p):
                rows = bass.AP(x_table.tensor, x_table.offset + VIEW_START[v] * BATCH * DIMS + column,
                               [[BATCH * DIMS, FIELDS], [VIEW_STEP[v] * BATCH * DIMS, LANES], [1, STEP_COLS]])
                sp.dma_start(views[p][:, v, :], rows).then_inc(views_loaded[p][v], 16)

            def load_factors(step, p):
                sp.dma_start(factors[p][:, :, :].rearrange("p k c -> p (k c)"), x_last[step, :, :])\
                    .then_inc(factors_loaded[p], 16)

            def load_x_by_dim(step):
                sp.dma_start(x_by_dim[:, bass.ds(step, 2), :, :].rearrange("p s g h -> p (s g h)"),
                             x_dims[:, bass.ds(step * P, 2 * P)]).then_inc(x_by_dim_loaded, 16)

            def load_w1(i):
                sp.dma_start(w1_sb[:, bass.ds(i * W1_FIELDS, W1_FIELDS), :],
                             w1[:, bass.ds(i * W1_FIELDS, W1_FIELDS), :]).then_inc(w1_loaded, 16)

            def load_step(step, p):
                used = (step - 2) * Z_OPS
                sp.wait_ge(z_made, used + 2).then_inc(sp_turns, 1)
                for v in (1, 2):
                    load_view(v, step * STEP_COLS, p)
                sp.wait_ge(z_made, used + 3).then_inc(sp_turns, 1)
                for v in (0, 3):
                    load_view(v, step * STEP_COLS, p)
                sp.wait_ge(z_made, used + 4).then_inc(sp_turns, 1)
                load_factors(step, p)
                if p == 0:
                    sp.wait_ge(x_by_dim_loaded, step * 8).then_inc(sp_turns, 1)
                    load_x_by_dim(step)

            def load_weights(target, source, loaded):
                sp.dma_start(target, source).then_inc(loaded, 16)

            for v in (1, 2):
                load_view(v, 0, 0)
            load_weights(w0_tile3_sb[:, :, :].rearrange("p u j -> p (u j)"), w0_tile3, w0_tile3_loaded)
            load_view(0, 0, 0)
            load_weights(w0_rest_sb[:, :], w0_rest, w0_rest_loaded)
            load_view(3, 0, 0)
            load_factors(0, 0)
            load_weights(w0_last_sb[:, :, :].rearrange("p u j -> p (u j)"), w0_last, w0_last_loaded)
            for v in (1, 2, 0, 3):
                load_view(v, STEP_COLS, 1)
            load_factors(1, 1)
            load_x_by_dim(0)
            load_step(2, 0)
            load_step(3, 1)
            load_w1(0)
            with sp.Fori(2, 1 + W1_LOADS // 2) as i:
                for p in range(2):
                    load_step(i * 2 + p, p)
                    load_w1(i * 2 + p - 3)
            load_w1(W1_LOADS - 1)
            with sp.Fori(1 + W1_LOADS // 2, STEPS // 2) as i:
                for p in range(2):
                    load_step(i * 2 + p, p)

        @block.gpsimd
        def _(pool):
            pool.memset(table_data[:, :], 0.0).then_inc(table_input, 1)
            pool.memset(zeros[:, :], 0.0).then_inc(zeros_made, 1)
            pool.memset(w0_last_terms[:, :, :].bitcast(F32), 0.0).then_inc(w0_cleared, 1)
            pool.memset(ident[:, :], 0.0).then_inc(constants_made, 1)
            for p in range(2):
                pool.memset(xblock[p][:, :, :, :], 0.0).then_inc(constants_made, 1)
            pool.wait_ge(constants_made, 3)
            pool.affine_select(out=ident[:, :], in_=ident[:, :], compare_op=ALU.not_equal, fill=1.0,
                               base=0, pattern=[[-1, P]], channel_multiplier=1).then_inc(constants_made, 1)
            for p in range(2):
                for b in range(GROUP_B):
                    pool.wait_ge(constants_made, 4 + p * GROUP_B + b)
                    pool.memset(xblock[p][b * DIMS:(b + 1) * DIMS, :, FIELDS, b:b + 1], 1.0)\
                        .then_inc(constants_made, 1)

        @block.vector
        def _(dve):
            def constant(which, rows=slice(0, P)):
                return w0_rest_sb[rows, W0_CONSTANTS + which:W0_CONSTANTS + which + 1]

            def tile3_products(p):
                dve.tensor_tensor(z[p][:, 3, :], views[p][:, 1, :], views[p][:, 2, :], ALU.mult).then_inc(z_made, 1)

            def tiles01_products(p, i):
                dve.wait_ge(views_loaded[p][0], (i + 1) * 16)
                dve.tensor_tensor(z[p][:, 0:2, :], views[p][:, 0:1, :].broadcast_to([P, 2, STEP_COLS]),
                                  views[p][:, 1:3, :], ALU.mult).then_inc(z_made, 1)

            def other_products(p, i):
                dve.wait_ge(views_loaded[p][3], (i + 1) * 16)
                dve.tensor_tensor(z[p][:, 2, :], views[p][:, 0, :], views[p][:, 3, :], ALU.mult).then_inc(z_made, 1)
                dve.wait_ge(factors_loaded[p], (i + 1) * 16)
                dve.tensor_tensor(z_last[p][:, :], factors[p][:, 0, :], factors[p][:, 1, :], ALU.mult)\
                    .then_inc(z_made, 1)

            def wait_for_views12(p, i):
                for v in (1, 2):
                    dve.wait_ge(views_loaded[p][v], (i + 1) * 16)

            def products(step, p, i, whole=False):
                wait_for_views12(p, i)
                if whole:
                    dve.wait_ge(z_whole_used, step - 1)
                tiles01_products(p, i)
                if not whole:
                    dve.wait_ge(z_whole_used, step - 1)
                tile3_products(p)
                other_products(p, i)

            def lows(step, p, split):
                if split > 0:
                    dve.wait_ge(z_highs, step * PARTS + 1)
                    dve.tensor_tensor(z_low[p][:, 0:2, :], z[p][:, 0:2, :], z_high[p][:, 0:2, :].bitcast(F32),
                                      ALU.subtract).then_inc(z_lows, 2 if split == 2 else 1)
                if split == 3:
                    dve.wait_ge(z_highs, step * PARTS + 2)
                    dve.tensor_tensor(z_low[p][:, 2, :], z[p][:, 2, :], z_high[p][:, 2, :].bitcast(F32),
                                      ALU.subtract).then_inc(z_lows, 1)
                dve.wait_ge(z_highs, step * PARTS + PARTS)
                dve.scalar_tensor_tensor(out=z_last_terms[p][:, :], in0=z_last_high[p][:, :].bitcast(F32),
                                         scalar=constant(SIGN_Z), in1=z_last[p][:, :], op0=ALU.mult, op1=ALU.add)\
                    .then_inc(z_lows, PARTS if split == 0 else 1)

            def fold_tile3_weights():
                dve.wait_ge(w0_tile3_loaded, 16)
                dve.tensor_tensor(w0_tile3_sum[:, :], w0_tile3_sb[:, 0, :], w0_tile3_sb[:, 1, :], ALU.add)\
                    .then_inc(w0_tile3_folded, 1)

            def fold_weights():
                dve.wait_ge(w0_rest_loaded, 16)
                both = w0_rest_sb[:, 0:W0_CONSTANTS].rearrange("p (u t j) -> p u t j", u=2, j=J)
                dve.tensor_tensor(w0_sum[:, :, :], both[:, 0, :, :], both[:, 1, :, :], ALU.add).then_inc(w0_added, 1)
                dve.wait_ge(w0_added, 1)
                dve.tensor_scalar(w0_sum[:, DIAGONAL, :], w0_sum[:, DIAGONAL, :], constant(ONCE), None, ALU.mult)\
                    .then_inc(w0_folded, 1)

            def fold_last_weights():
                dve.wait_ge(w0_last_loaded, 16)
                dve.tensor_tensor(w0_last_sum[:, :], w0_last_sb[:, 0, :], w0_last_sb[:, 1, :], ALU.add)\
                    .then_inc(w0_last_folded, 1)

            def last_weight_terms():
                dve.wait_ge(w0_cleared, 1)
                dve.wait_ge(w0_highs, 1)
                for half in range(HALVES):
                    rows = slice(half * LAST_ROWS, (half + 1) * LAST_ROWS)
                    dve.scalar_tensor_tensor(out=w0_last_terms[rows, half, :], in0=w0_last_high[rows, :].bitcast(F32),
                                             scalar=constant(SIGN_W, rows), in1=w0_last_sum[rows, :],
                                             op0=ALU.mult, op1=ALU.add).then_inc(w0_lows, 1)

            def weight_lows():
                dve.wait_ge(w0_highs, 2)
                dve.tensor_tensor(w0_low[:, :, :], w0_sum[:, :, :], w0_high[:, :, :].bitcast(F32),
                                  ALU.subtract).then_inc(w0_lows, 1)

            wait_for_views12(0, 0)
            tile3_products(0)
            fold_tile3_weights()
            tiles01_products(0, 0)
            fold_weights()
            other_products(0, 0)
            fold_last_weights()
            lows(0, 0, 0)
            last_weight_terms()
            wait_for_views12(1, 0)
            tile3_products(1)
            tiles01_products(1, 0)
            other_products(1, 0)
            weight_lows()
            lows(1, 1, 0)

            def pair(i, whole=False):
                for p in range(2):
                    products(i * 2 + p, p, i, whole=whole)
                    lows(i * 2 + p, p, SPLITS[p])

            pair(1, whole=True)
            with dve.Fori(2, STEPS // 2) as i:
                pair(i)

        @block.scalar
        def _(act):
            act.wait_ge(table_input, 1)
            act.activation(table_data[:, 1:2], table_data[:, 0:1], ACT.Copy).then_inc(table_ready, 1)
            act.wait_ge(table_ready, 1)

            def highs01(step, p, split):
                act.wait_ge(z_made, step * Z_OPS + 1)
                act.activation(z_high[p][:, 0:2, :], z[p][:, 0:2, :], ACT.Copy)\
                    .then_inc(z_highs, 2 if split == 2 else 1)

            def other_highs(step, p, split):
                if split == 3:
                    act.wait_ge(z_made, step * Z_OPS + 3)
                    act.activation(z_high[p][:, 2, :], z[p][:, 2, :], ACT.Copy).then_inc(z_highs, 1)
                act.wait_ge(z_made, step * Z_OPS + Z_OPS)
                act.activation(z_last_high[p][:, :], z_last[p][:, :], ACT.Copy)\
                    .then_inc(z_highs, PARTS if split == 0 else 1)

            def x1_copy(step, p):
                act.wait_ge(x1_done, step + 1)
                act.activation(x1_sb[:, :], x1_ps[p][:, :], ACT.Copy).then_inc(x1_copied, 1)

            def turned_copy(step):
                act.wait_ge(x1_was_turned, step + 1)
                act.activation(x1_turned[:, :, :], turned_ps[:, :, :], ACT.Copy).then_inc(turned_copied, 1)

            def block_diagonal(step, p):
                act.wait_ge(x_by_dim_loaded, (step - p) * 8 + 16)
                for b in range(GROUP_B):
                    rows = slice(b * DIMS, (b + 1) * DIMS)
                    act.activation(xblock[p][rows, :, 0:FIELDS, b],
                                   x_by_dim[rows, bass.ds(step, 1), :, :].rearrange("p s g h -> p (s g) h"),
                                   ACT.Copy).then_inc(xblock_made, 1)

            def g_copies(step, chunk_step):
                for k in range(2):
                    act.wait_ge(g_done, step * 2 + k + 1)
                    source = g_ps[k][:, 0:2 * GCOLS].rearrange("p (g h b) -> p h g b", g=2, b=GROUP_B)
                    target = g_sb[:, :, bass.ds(chunk_step * STEP_B + k * 2 * GROUP_B, 2 * GROUP_B)]
                    act.activation(target.rearrange("p h (g b) -> p h g b", g=2), source, ACT.Copy)\
                        .then_inc(g_copied, 1)

            def store(c, first=False):
                act.wait_ge(out_done, c + 1)
                if not first:
                    act.wait_ge(out_stored, c * 16)
                act.activation(out_sb[:, :], out_ps[:, 0:2 * J], ACT.Copy).then_inc(out_copied, 1)
                act.wait_ge(out_copied, c + 1)
                act.dma_start(out[bass.ds(c * CHUNK_B, CHUNK_B), :], out_sb[:, :]).then_inc(out_stored, 16)

            def turn(step, p, chunk_step, finished=None, first=False, behind=False):
                split = SPLITS[1 - p]
                x1_copy(step - 1, 1 - p)
                if not behind:
                    highs01(step + 1, 1 - p, split)
                if finished is not None:
                    other_highs(step + 1, 1 - p, split)
                    store(finished, first)
                g_copies(step - 2, chunk_step)
                turned_copy(step - 1)
                if behind:
                    highs01(step + 1, 1 - p, split)
                if finished is None:
                    other_highs(step + 1, 1 - p, split)
                block_diagonal(step, p)

            def chunk_start(c, first=False):
                turn(c * CHUNK_STEPS + 2, 0, 0, finished=c - 1, first=first)
                turn(c * CHUNK_STEPS + 3, 1, 1)

            def chunk_pairs(c, begin, end, behind=False):
                with act.Fori(begin, end) as i:
                    for p in range(2):
                        turn(c * CHUNK_STEPS + i * 2 + p + 2, p, i * 2 + p, behind=behind)

            other_highs(0, 0, 0)
            act.wait_ge(w0_last_folded, 1)
            act.activation(w0_last_high[:, :], w0_last_sum[:, :], ACT.Copy).then_inc(w0_highs, 1)
            act.wait_ge(w0_folded, 1)
            act.activation(w0_high[:, :, :], w0_sum[:, :, :], ACT.Copy).then_inc(w0_highs, 1)
            act.wait_ge(constants_made, CONSTANTS)
            other_highs(1, 1, 0)
            block_diagonal(0, 0)
            x1_copy(0, 0)
            turned_copy(0)
            highs01(2, 0, SPLITS[0])
            other_highs(2, 0, SPLITS[0])
            block_diagonal(1, 1)
            chunk_pairs(0, 0, 1, behind=True)
            chunk_pairs(0, 1, PAIRS)
            chunk_start(1, first=True)
            chunk_pairs(1, 1, PAIRS)
            with act.Fori(2, CHUNKS - 1) as c:
                chunk_start(c)
                chunk_pairs(c, 1, PAIRS)
            chunk_start(CHUNKS - 1)
            chunk_pairs(CHUNKS - 1, 1, PAIRS - 2)
            turn(STEPS - 2, 0, CHUNK_STEPS - 4)
            x1_copy(STEPS - 2, 0)
            g_copies(STEPS - 3, CHUNK_STEPS - 3)
            turned_copy(STEPS - 2)
            block_diagonal(STEPS - 1, 1)
            act.wait_ge(x1_done, STEPS)
            act.wait_ge(x1_was_turned, STEPS - 1)
            for half in range(HALVES):
                columns = slice(half * LAST_COLS, (half + 1) * LAST_COLS)
                act.activation(x1_sb[:, columns], x1_ps[1][:, columns], ACT.Copy).then_inc(x1_copied, 1)
            g_copies(STEPS - 2, CHUNK_STEPS - 2)
            for half in range(HALVES):
                act.wait_ge(x1_was_turned, STEPS + half)
                act.activation(x1_turned[:, half * HALF_GROUPS:(half + 1) * HALF_GROUPS, :],
                               turned_half_ps[half], ACT.Copy).then_inc(turned_copied, 1)
            g_copies(STEPS - 1, CHUNK_STEPS - 1)
            store(CHUNKS - 1)
            act.wait_ge(out_stored, 16 * CHUNKS)

        @block.tensor
        def _(pe):
            def split_tile(x1, p, t):
                pe.matmul(x1, w0_high[:, t, :], z_low[p][:, t, :], start=False, stop=False)
                pe.matmul(x1, w0_low[:, t, :], z_high[p][:, t, :], start=False, stop=False)
                pe.matmul(x1, w0_high[:, t, :], z_high[p][:, t, :], start=False, stop=False)

            def whole_tile(p, t, first=False):
                weights = w0_tile3_sum[:, :] if t == 3 else w0_sum[:, t, :]
                return pe.matmul(x1_ps[p][:, :], weights, z[p][:, t, :], start=first, stop=False)

            def layer0_begin(step, p, split):
                pe.wait_ge(z_made, step * Z_OPS + 2)
                last = whole_tile(p, 3, first=True)
                if split == 2:
                    pe.wait_ge(z_made, step * Z_OPS + 3)
                    last = whole_tile(p, 2)
                last.then_inc(z_whole_used, 1)

            def last_shift(step, p):
                pe.wait_ge(z_lows, step * PARTS + PARTS)
                for half in range(HALVES):
                    last = pe.matmul(x1_ps[p][:, half * LAST_COLS:(half + 1) * LAST_COLS], w0_last_terms[:, half, :],
                                     z_last_terms[p][:, :], start=False, stop=(half == HALVES - 1))
                last.then_inc(x1_done, 1)

            def layer0_end(step, p, split):
                pe.wait_ge(z_lows, step * PARTS + 1)
                split_tile(x1_ps[p][:, :], p, 0)
                split_tile(x1_ps[p][:, :], p, 1)
                if split == 3:
                    pe.wait_ge(z_lows, step * PARTS + 2)
                    split_tile(x1_ps[p][:, :], p, 2)
                last_shift(step, p)

            def layer0_of_first_step():
                pe.wait_ge(w0_tile3_folded, 1)
                pe.wait_ge(z_made, 1)
                whole_tile(0, 3, first=True)
                pe.wait_ge(w0_folded, 1)
                pe.wait_ge(z_made, 2)
                whole_tile(0, 0)
                whole_tile(0, 1)
                pe.wait_ge(z_made, 3)
                whole_tile(0, 2).then_inc(z_whole_used, 1)
                pe.wait_ge(w0_lows, HALVES)
                last_shift(0, 0)

            def layer0_of_second_step():
                pe.wait_ge(z_made, Z_OPS + 1)
                whole_tile(1, 3, first=True)
                pe.wait_ge(z_made, Z_OPS + 2)
                whole_tile(1, 0)
                whole_tile(1, 1)
                pe.wait_ge(z_made, Z_OPS + 3)
                whole_tile(1, 2).then_inc(z_whole_used, 1)
                last_shift(1, 1)

            def turn_group(target, g):
                return pe.transpose(target, x1_sb[:, g * P:(g + 1) * P], ident[:, :])

            def turn_x1(step):
                pe.wait_ge(x1_copied, step + 1)
                for g in range(STEP_GROUPS):
                    last = turn_group(turned_ps[:, g, :], g)
                last.then_inc(x1_was_turned, 1)

            def gram(p, k):
                for g in range(k * HALF_GROUPS, (k + 1) * HALF_GROUPS):
                    column = (g % HALF_GROUPS) * GCOLS
                    last = pe.matmul(g_ps[k][:, column:column + GCOLS], x1_turned[:, g, :],
                                     xblock[p][:, g, :, :].rearrange("p h b -> p (h b)"), start=True, stop=True)
                last.then_inc(g_done, 1)

            def layer1_gram(step, p, first=False):
                pe.wait_ge(xblock_made, (step + 1) * GROUP_B)
                pe.wait_ge(turned_copied, step + 1)
                for k in range(2):
                    if not first:
                        pe.wait_ge(g_copied, step * 2 - 1 + k)
                    gram(p, k)

            def layer1_of_last_step():
                for half in range(HALVES):
                    pe.wait_ge(x1_copied, STEPS + half)
                    for g in range(HALF_GROUPS):
                        last = turn_group(turned_half_ps[half][:, g, :], half * HALF_GROUPS + g)
                    last.then_inc(x1_was_turned, 1)
                pe.wait_ge(xblock_made, STEPS * GROUP_B)
                for half in range(HALVES):
                    pe.wait_ge(turned_copied, STEPS + half)
                    pe.wait_ge(g_copied, STEPS * 2 - 3 + half)
                    gram(1, half)

            def output(c, first=False):
                pe.wait_ge(g_copied, (c + 1) * (2 * CHUNK_STEPS))
                if first:
                    pe.wait_ge(w1_loaded, 16 * W1_LOADS)
                else:
                    pe.wait_ge(out_copied, c)
                pe.matmul(out_ps[:, 0:J], g_sb[:, FIELDS, :], ident[:, :], start=True, stop=True)
                for h in range(FIELDS):
                    last = pe.matmul(out_ps[:, J:2 * J], g_sb[:, h, :], w1_sb[:, h, :],
                                     start=(h == 0), stop=(h == FIELDS - 1))
                last.then_inc(out_done, 1)

            def turn(step, p, split, finished=None, first=False):
                layer0_begin(step, p, split)
                turn_x1(step - 1)
                layer0_end(step, p, split)
                if finished is not None:
                    output(finished, first)
                layer1_gram(step - 1, 1 - p)

            def chunk_start(c, first=False):
                turn(c * CHUNK_STEPS, 0, SPLITS[0])
                turn(c * CHUNK_STEPS + 1, 1, SPLITS[1], finished=c - 1, first=first)

            def chunk_rest(c):
                with pe.Fori(1, PAIRS) as i:
                    for p in range(2):
                        turn(c * CHUNK_STEPS + i * 2 + p, p, SPLITS[p])

            pe.wait_ge(zeros_made, 1)
            for _ in range(WARM_PRODUCTS):
                pe.matmul(out_ps[:, 0:WARM_COLS], zeros[:, 0:P], zeros[:, :], start=True, stop=True)
            layer0_of_first_step()
            layer0_of_second_step()
            pe.wait_ge(constants_made, CONSTANTS)
            turn_x1(0)
            layer1_gram(0, 0, first=True)
            pe.wait_ge(w0_lows, HALVES + 1)
            chunk_rest(0)
            chunk_start(1, first=True)
            chunk_rest(1)
            with pe.Fori(2, CHUNKS) as c:
                chunk_start(c)
                chunk_rest(c)
            layer1_of_last_step()
            output(CHUNKS - 1)


def kernel(r_inputs, L0_rec_W0, L0_rec_W1):
    import numpy as np
    import concourse.bacc as bacc
    from concourse.bass_utils import run_bass_kernel_spmd

    x = np.ascontiguousarray(r_inputs)
    x_rows = x.transpose(1, 0, 2).reshape(FIELDS, BATCH * DIMS)
    table = x_rows[[f % FIELDS for f in range(TABLE_ROWS)]]
    grouped = x.reshape(STEPS, HALVES, STEP_GROUPS // HALVES, GROUP_B, FIELDS, DIMS)
    by_field = grouped.transpose(0, 1, 4, 2, 3, 5).reshape(STEPS, HALVES, 1, FIELDS, LAST_COLS)
    shape = (STEPS, HALVES, TERMS, LAST_PAIRS, LAST_COLS)
    factor = np.broadcast_to(by_field[:, :, :, :LAST_PAIRS], shape)
    partner = np.broadcast_to(by_field[:, :, :, LAST_PAIRS:], shape)
    x_by_dim = x.reshape(STEPS, STEP_GROUPS, GROUP_B, FIELDS, DIMS).transpose(2, 4, 0, 1, 3)
    w0 = np.asarray(L0_rec_W0)
    rows = [(r, lane) for r in range(FIELDS) for lane in range(LANES)]
    def pairs(tiles, turned):
        fields = [[(field_of(a, r, lane), field_of(b, r, lane)) for a, b in tiles] for r, lane in rows]
        return w0[[[m * FIELDS + h if turned else h * FIELDS + m for h, m in row] for row in fields]]

    last = [[i * FIELDS + i + LAST_PAIRS, (i + LAST_PAIRS) * FIELDS + i]
            for _ in range(HALVES * TERMS) for i in range(LAST_PAIRS)]
    row_constants = np.zeros((P, 3), np.float32)
    for row, (half, term, pair) in enumerate(np.ndindex(HALVES, TERMS, LAST_PAIRS)):
        row_constants[row, SIGN_Z] = -(term // 2)
        row_constants[row, SIGN_W] = -(term % 2)
        row_constants[row, ONCE] = 0.5 if row % LANES == 0 else 1.0
    both = [pairs(TILE_VIEWS[:REST_TILES], False), pairs(TILE_VIEWS[:REST_TILES], True)]
    rest = [a.reshape(P, REST_TILES * J) for a in both] + [row_constants]
    tile3 = [pairs(TILE_VIEWS[REST_TILES:], turned).reshape(P, J) for turned in (False, True)]
    arrays = {
        "x_table": table,
        "x_last": np.concatenate([a.reshape(STEPS, P, LAST_COLS) for a in (factor, partner)], axis=2),
        "x_dims": x_by_dim.reshape(P, STEPS * P),
        "w0_tile3": np.concatenate(tile3, axis=1),
        "w0_rest": np.concatenate(rest, axis=1),
        "w0_last": w0[last].reshape(P, 2 * J),
        "w1": np.asarray(L0_rec_W1).reshape(FIELDS, P, J).transpose(1, 0, 2),
    }
    arrays = {name: np.ascontiguousarray(a) for name, a in arrays.items()}

    nc = bacc.Bacc("TRN2", target_bir_lowering=False, num_devices=1)
    args = [nc.dram_tensor(name, a.shape, F32, kind="ExternalInput").ap() for name, a in arrays.items()]
    out = nc.dram_tensor("out", (BATCH, 2 * J), F32, kind="ExternalOutput").ap()
    cin_kernel(nc, *args, out)
    result = run_bass_kernel_spmd(nc, [arrays], core_ids=[0])
    return result.results[0]["out"]
```
